# Optimizing a Trainium2 kernel written in Bass

```python
import numpy as np
import jax
import jax.numpy as jnp

def _softmax(x, axis=-1):
    return jax.nn.softmax(x, axis=axis)

def _gelu(x):
    return jax.nn.gelu(x, approximate=True)

def _silu(x):
    return jax.nn.silu(x)

def _sigmoid(x):
    return jax.nn.sigmoid(x)

def _layernorm(x, axis=-1, eps=1e-05):
    m = jnp.mean(x, axis=axis, keepdims=True)
    v = jnp.var(x, axis=axis, keepdims=True)
    return (x - m) / jnp.sqrt(v + eps)

def _scatter_add(tgt, idx, src, axis=0):
    return tgt.at[idx].add(src)

def _segment_sum(src, seg, n):
    return jax.ops.segment_sum(src, seg, n)
kernel_name = 'mk_cond_resid_d2_seqx_r4_eb8187'

def setup_inputs(seed: int=0):
    np.random.seed(seed)
    _w = jnp.asarray

    def _rec_inputs():
        import jax
        import jax.numpy as jnp
        _rk = jax.random.key(seed)
        x = -0.0003929 + 0.9999 * jax.random.normal(jax.random.fold_in(_rk, 1), (16, 256, 256), jnp.float32)
        _lenS = 256 - jax.random.randint(jax.random.fold_in(_rk, 7), (16,), 0, max(1, 256 // 4) + 1, jnp.int32)
        _lenS2 = 256 - jax.random.randint(jax.random.fold_in(_rk, 8), (16,), 0, max(1, 256 // 4) + 1, jnp.int32)
        cond_1024 = 0.00061147 + 0.102565 * jax.random.normal(jax.random.fold_in(_rk, 11), (16, 256), jnp.float32)
        return (x, cond_1024)
    x, cond_1024 = _rec_inputs()

    def _L0_cond_setup():
        import jax, jax.numpy as jnp
        import numpy as np
        key = jax.random.key(seed)
        ks = jax.random.split(key, 8)
        B, L, D, N, K = (4, 1024, 256, 64, 4)
        return {'x': jax.random.normal(ks[0], (B, L, D), dtype=jnp.float32), 'conv_w': jax.random.normal(ks[1], (K, 1, D), dtype=jnp.float32) * 0.1, 'conv_b': jnp.zeros((D,), dtype=jnp.float32), 'Wp': jax.random.normal(ks[2], (D, 2 * N), dtype=jnp.float32) * (1.0 / np.sqrt(D)), 'bp': jnp.zeros((2 * N,), dtype=jnp.float32), 'Ws': jax.random.normal(ks[3], (D, N), dtype=jnp.float32) * (1.0 / np.sqrt(D)), 'bs': jnp.zeros((N,), dtype=jnp.float32), 'A_log': jax.random.normal(ks[4], (N,), dtype=jnp.float32) * 0.02, 'dt_log': jax.random.normal(ks[5], (N,), dtype=jnp.float32) * 0.02, 'Wo': jax.random.normal(ks[6], (N, D), dtype=jnp.float32) * (1.0 / np.sqrt(N)), 'bo': jnp.zeros((D,), dtype=jnp.float32)}
    _L0_cond_all = _L0_cond_setup()
    _L0_cond_in = {k: v for k, v in _L0_cond_all.items() if k in ('conv_b', 'Wp', 'bp', 'Ws', 'bs', 'A_log', 'dt_log', 'Wo', 'bo')}
    del _L0_cond_all

    def _L1_cond_setup():
        import jax, jax.numpy as jnp
        import numpy as np
        import math
        N, T, D, H = (128, 128, 256, 256)
        key = jax.random.key(seed)
        k1, k2, k3, k4 = jax.random.split(key, 4)
        x = jax.random.normal(k1, (N, T, D), dtype=jnp.float32)
        h0 = jax.random.normal(k2, (N, H), dtype=jnp.float32)
        Wx = jax.random.normal(k3, (D, H), dtype=jnp.float32) / math.sqrt(D)
        Wh = jax.random.normal(k4, (H, H), dtype=jnp.float32) / math.sqrt(H)
        b = jnp.zeros((H,), dtype=jnp.float32)
        return {'x': x, 'h0': h0, 'Wx': Wx, 'Wh': Wh, 'b': b}
    _L1_cond_all = _L1_cond_setup()
    _L1_cond_in = {k: v for k, v in _L1_cond_all.items() if k in ('Wx', 'Wh', 'b')}
    del _L1_cond_all
    return {'x': x, 'cond_1024': cond_1024, 'L0_cond_conv_b': _L0_cond_in['conv_b'], 'L0_cond_Wp': _L0_cond_in['Wp'], 'L0_cond_bp': _L0_cond_in['bp'], 'L0_cond_Ws': _L0_cond_in['Ws'], 'L0_cond_bs': _L0_cond_in['bs'], 'L0_cond_A_log': _L0_cond_in['A_log'], 'L0_cond_dt_log': _L0_cond_in['dt_log'], 'L0_cond_Wo': _L0_cond_in['Wo'], 'L0_cond_bo': _L0_cond_in['bo'], 'L1_cond_Wx': _L1_cond_in['Wx'], 'L1_cond_Wh': _L1_cond_in['Wh'], 'L1_cond_b': _L1_cond_in['b']}

def reference(x, cond_1024, L0_cond_conv_b, L0_cond_Wp, L0_cond_bp, L0_cond_Ws, L0_cond_bs, L0_cond_A_log, L0_cond_dt_log, L0_cond_Wo, L0_cond_bo, L1_cond_Wx, L1_cond_Wh, L1_cond_b):
    import jax
    import jax.numpy as jnp

    def _L0_cond_ref(x, conv_w, conv_b, Wp, bp, Ws, bs, A_log, dt_log, Wo, bo):
        import jax, jax.numpy as jnp
        import numpy as np
        B, L, D = x.shape
        K = conv_w.shape[0]
        N = Ws.shape[1]
        x_pad = jnp.pad(x, ((0, 0), (K - 1, 0), (0, 0)))
        conv = conv_b + sum((x_pad[:, k:k + L, :] * conv_w[k, 0] for k in range(K)))
        proj = conv @ Wp + bp
        B_t = jax.nn.softplus(proj[..., :N])
        C_t = jnp.tanh(proj[..., N:])
        u = x @ Ws + bs
        A = -jax.nn.softplus(A_log)
        dt = jax.nn.softplus(dt_log)
        decay = 1.0 + dt * A

        def step(state, inputs):
            u_t, b_t, c_t = inputs
            state = decay * state + dt * b_t * u_t
            return (state, c_t * state)
        init = jnp.zeros((B, N), dtype=x.dtype)
        xs = tuple((jnp.swapaxes(a, 0, 1) for a in (u, B_t, C_t)))
        _, ys = jax.lax.scan(step, init, xs, unroll=4)
        y = jnp.swapaxes(ys, 0, 1)
        return y @ Wo + bo

    def _L1_cond_ref(x, h0, Wx, Wh, b):
        import jax, jax.numpy as jnp
        import numpy as np
        import math
        N, T, D, H = (128, 128, 256, 256)
        xW = jnp.einsum('ntd,dh->nth', x, Wx) + b

        def step(h_prev, xw_t):
            h_next = jnp.tanh(h_prev @ Wh + xw_t)
            return (h_next, h_next)
        _, hs = jax.lax.scan(step, h0, jnp.swapaxes(xW, 0, 1))
        return jnp.swapaxes(hs, 0, 1)
    x = x + _L0_cond_ref(x, cond_1024[:, None, :], L0_cond_conv_b, L0_cond_Wp, L0_cond_bp, L0_cond_Ws, L0_cond_bs, L0_cond_A_log, L0_cond_dt_log, L0_cond_Wo, L0_cond_bo)
    x = x + _L1_cond_ref(x, cond_1024, L1_cond_Wx, L1_cond_Wh, L1_cond_b)
    return x

_drawn_inputs = setup_inputs


def setup_inputs(seed=0):
    import zlib

    import numpy as np

    out = dict(_drawn_inputs(seed))
    spreads = {'L0_cond_conv_b': (0.0, 0.1),
     'L0_cond_bp': (0.0, 0.1),
     'L0_cond_bs': (0.0, 0.1),
     'L0_cond_bo': (0.0, 0.1),
     'L1_cond_b': (0.0, 0.1)}
    factors = {'L0_cond_A_log': 22.436, 'L0_cond_dt_log': 8.0}
    for name, (base, spread) in spreads.items():
        noise = np.random.default_rng([zlib.crc32(name.encode()), seed]).standard_normal(out[name].shape)
        drawn = base * np.exp(spread * noise) if base else spread * noise
        out[name] = jnp.asarray(drawn.astype(out[name].dtype))
    for name, factor in factors.items():
        out[name] = (out[name] * factor).astype(out[name].dtype)
    return out
```

```python
import concourse.bass as bass
from concourse import mybir
from contextlib import ExitStack

FP32 = mybir.dt.float32
BF16 = mybir.dt.bfloat16
ACT = mybir.ActivationFunctionType
ALU = mybir.AluOpType

LOG1P = [1.0, -0.49999502301216125, 0.33319270610809326, -0.24844369292259216, 0.19111430644989014,
         -0.13674770295619965, 0.07836166769266129, -0.02958850748836994, 0.005253457929939032]


class Chunk:

    def __init__(self, lap, at):
        self.lap, self.at = lap, at

    def __add__(self, d):
        return Chunk(self.lap, self.at + d)

    def count(self, per_chunk, plus):
        v = per_chunk * self.at + plus
        return v if isinstance(self.lap, int) else self.lap * (4 * per_chunk) + v

    def laps(self, per_lap, plus=0):
        v = per_lap * (self.at // 4 + 1 + plus)
        return v if isinstance(self.lap, int) else self.lap * per_lap + v

    @property
    def slot(self):
        return self.at % 4

    @property
    def pair(self):
        return self.at % 2


def build(nc, x, cond, conv_b, Wp, bp, Ws, bs, A_log, dt_log, Wo, bo, Wx, Wh, b, out):
    B, L, D = x.shape
    N = Ws.shape[1]
    TAPS = B
    P = 128
    HALVES = D // P
    STEPS = 16
    COLS = STEPS * B
    CHUNKS = L // STEPS
    RING = 4
    HALO = (TAPS - 1) * B
    TILE_T = P // B
    TILES = COLS // P
    BH = B // 2
    POOL_TAPS = 8
    FIRST_LOOPED, LAPS = 1, 3
    assert CHUNKS == FIRST_LOOPED + RING * LAPS + 3 and 2 * N == P and TILES == 2 and HALVES == 2

    ctx = ExitStack()
    with ctx:
        def sb(name, shape, dt=FP32):
            return ctx.enter_context(nc.sbuf_tensor(name, shape, dt))

        def pb(name, shape):
            return ctx.enter_context(nc.psum_tensor(name, shape, FP32))

        def sem(name):
            return ctx.enter_context(nc.semaphore(name))

        Wp_sb = sb("Wp_sb", [P, HALVES, 2 * N])
        Ws_sb = sb("Ws_sb", [P, HALVES, N])
        Wx_sb = sb("Wx_sb", [P, HALVES, D])
        Wh_sb = sb("Wh_sb", [P, HALVES, D])
        Wh_rest = sb("Wh_rest", [P, HALVES, D])
        Wh_parts = sb("Wh_parts", [P, 3, HALVES, D], BF16)
        Wo_bo = sb("Wo_bo", [N + 1, D])
        Wo_boT = sb("Wo_boT", [P, HALVES, N + 1])
        Wox = sb("Wox", [N + 1, D])
        b_row = sb("b_row", [N + 1, D])
        cond_sb = sb("cond_sb", [B, D])
        taps = sb("taps", [P, HALVES, TAPS])
        conv_bT = sb("conv_bT", [P, HALVES])
        bp_col = sb("bp_col", [P, 1])
        bs_col = sb("bs_col", [P, 1])
        logs = sb("logs", [P, 2])
        logs_abs = sb("logs_abs", [P, 2])
        logs_exp = sb("logs_exp", [P, 2])
        logs_sp = sb("logs_sp", [P, 2])
        dt_A = sb("dt_A", [P, 1])
        decay = sb("decay", [P, 1])
        decays = sb("decays", [P, BH, STEPS])
        ident = sb("ident", [P, P])
        x_rows = sb("x_rows", [P, RING, TILES, D])
        x_again = sb("x_again", [P, RING, TILES, D])
        xT = sb("xT", [P, HALVES, HALO + RING * COLS])
        products = sb("products", [P, 4, COLS])
        pool_conv = sb("pool_conv", [P, 2, HALVES, COLS])
        conv = sb("conv", [P, 2, HALVES, COLS])
        z_abs = sb("z_abs", [P, BH, STEPS])
        z_exp = sb("z_exp", [P, BH, STEPS])
        z_relu = sb("z_relu", [P, BH, STEPS])
        u_sb = sb("u_sb", [P, BH, STEPS])
        c_tanh = sb("c_tanh", [P, BH, STEPS])
        drive = sb("drive", [P, BH, STEPS])
        state = sb("state", [P, 2, BH, STEPS])
        yT = sb("yT", [N + 1, RING, COLS])
        hT = sb("hT", [P, RING, HALVES, COLS])
        h_rest = sb("h_rest", [P, 2, HALVES, B])
        h_last = sb("h_last", [P, 2, HALVES, B], BF16)
        out_rows = sb("out_rows", [P, RING, D])

        rec_ps = [pb(f"rec_ps{q}", [P, HALVES, 512]) for q in range(2)]
        xt_ps = pb("xt_ps", [P, 512])
        proj_ps = pb("proj_ps", [P, 512])
        out_ps = [pb(f"out_ps{j}", [P, 512]) for j in range(TILES)]

        w_in = {n: sem("in_" + n) for n in ("Wp", "Ws", "Wx", "Wh", "Wo", "bo", "b", "cond", "vec")}
        rows_in = [sem(f"rows_in{r}") for r in range(RING)]
        again_in = [sem(f"again_in{r}") for r in range(RING)]
        cleared = sem("cleared")
        ident_ready = sem("ident_ready")
        taps_ps_ready = sem("taps_ps_ready")
        taps_ready = sem("taps_ready")
        h0_ready = sem("h0_ready")
        WoT_ps_ready = sem("WoT_ps_ready")
        WoT_ready = sem("WoT_ready")
        Wox_ps_ready = sem("Wox_ps_ready")
        Wox_copied = sem("Wox_copied")
        Wox_ready = sem("Wox_ready")
        split = sem("split")
        consts = sem("consts")
        logs_act = sem("logs_act")
        xt_ps_ready = sem("xt_ps_ready")
        xt_ready = sem("xt_ready")
        halo_ready = sem("halo_ready")
        pool_step = sem("pool_step")
        product_ready = sem("product_ready")
        pool_base = [sem(f"pool_base{h}") for h in range(HALVES)]
        conv_step = [sem(f"conv_step{h}") for h in range(HALVES)]
        conv_ready = [sem(f"conv_ready{h}") for h in range(HALVES)]
        proj_ready = sem("proj_ready")
        proj_read = sem("proj_read")
        abs_ready = sem("abs_ready")
        exp_ready = sem("exp_ready")
        relu_ready = sem("relu_ready")
        u_ready = sem("u_ready")
        tanh_ready = sem("tanh_ready")
        tail_step = sem("tail_step")
        y_ready = sem("y_ready")
        mm_ready = sem("mm_ready")
        h_ready = sem("h_ready")
        rest_ready = sem("rest_ready")
        last_ready = sem("last_ready")
        out_ps_ready = sem("out_ps_ready")
        out_ready = sem("out_ready")
        stored = [sem(f"stored{r}") for r in range(RING)]

        block = ctx.enter_context(nc.Block())
        SPLITS = 5
        VECTORS = 9
        CHAIN = len(LOG1P) + 2 + 2

        def windows(eng, window):
            for w in range(FIRST_LOOPED):
                window(Chunk(0, w), w)
            with eng.Fori(0, LAPS) as lap:
                for w in range(RING):
                    window(Chunk(lap, FIRST_LOOPED + w), None)
            for w in range(CHUNKS - 3, CHUNKS):
                window(Chunk(0, w), w)

        PRODUCTS = HALVES * POOL_TAPS
        SUMS = HALVES * (POOL_TAPS - 1)

        def products_before(c, h, k):
            return lambda plus: (c + -1).count(SUMS, h * (POOL_TAPS - 1) + k - 1 + plus)

        def product_slot(c, h, k):
            return ((c.at - 1) * SUMS + h * (POOL_TAPS - 1) + k - 1) % 4

        def stores_before(c):
            v = 16 * (c.at // 2 + 1)
            return v if isinstance(c.lap, int) else c.lap * (16 * RING // 2) + v

        def exists(w, ahead):
            return w is None or 0 <= w + ahead < CHUNKS

        def rows_of(t, c, j):
            first = c.count(STEPS, TILE_T * j)
            return t[:, bass.ds(first, TILE_T), :].rearrange("b t d -> t b d")

        @block.sync
        def _(sp):
            def load(dst, c, done):
                for j in range(TILES):
                    sp.dma_start(dst[:, c.slot, j, :], rows_of(x, c, j)).then_inc(done[c.slot], 16)

            sp.dma_start(cond_sb[:, :], cond).then_inc(w_in["cond"], 16)
            load(x_rows, Chunk(0, 0), rows_in)
            sp.dma_start(Wp_sb[:, :, :], Wp.rearrange("(k p) n -> p k n", p=P)).then_inc(w_in["Wp"], 16)
            load(x_rows, Chunk(0, 1), rows_in)
            load(x_rows, Chunk(0, 2), rows_in)
            sp.dma_start(Wx_sb[:, :, :], Wx.rearrange("(k p) n -> p k n", p=P)).then_inc(w_in["Wx"], 16)
            load(x_again, Chunk(0, 0), again_in)

            def load_chunk(c):
                sp.wait_ge(xt_ps_ready, c.count(1, -RING + 1))
                load(x_rows, c, rows_in)
                sp.wait_ge(out_ready, c.count(TILES, -(RING - 1) * TILES))
                load(x_again, c, again_in)

            for n in range(1, RING):
                if n == RING - 1:
                    load(x_rows, Chunk(0, n), rows_in)
                load(x_again, Chunk(0, n), again_in)
            with sp.Fori(0, CHUNKS // RING - 1) as lap:
                for n in range(RING):
                    load_chunk(Chunk(lap, RING + n))
            for k in range(RING):
                sp.wait_ge(stored[k], 16 * (CHUNKS // 2 + 1))

        @block.gpsimd
        def _(pool):
            pool.memset(ident[:, :], 0.0).then_inc(ident_ready, 1)
            pool.wait_ge(ident_ready, 1)
            pool.affine_select(out=ident[:, :], in_=ident[:, :], compare_op=ALU.not_equal, fill=1.0,
                               base=0, pattern=[[-1, P]], channel_multiplier=1).then_inc(ident_ready, 1)
            def add_taps(c, i):
                h, k = divmod(i, POOL_TAPS)
                if k == 0:
                    return
                p = products_before(c, h, k)
                pool.wait_ge(product_ready, p(1))
                if k > 1:
                    pool.wait_ge(pool_step, p(0))
                else:
                    pool.wait_ge(pool_base[h], c.count(1, 0))
                acc = pool_conv[:, c.pair, h, :]
                ins = pool.tensor_tensor(acc, acc, products[:, product_slot(c, h, k), :], ALU.add)
                ins.then_inc(pool_step, 1)

            for n in (1, 2):
                for i in range(PRODUCTS):
                    add_taps(Chunk(0, n), i)

            def window(c, w):
                if exists(w, 3):
                    for i in range(PRODUCTS):
                        add_taps(c + 3, i)

            windows(pool, window)

        packed = [(0, slice(0, N)), (1, slice(N, P))]

        def unpacked(ap, half):
            return ap.rearrange("p (t b) -> p b t", b=B)[:, half * BH:(half + 1) * BH, :]

        @block.scalar
        def _(act):
            for h in range(HALVES):
                act.dma_start(conv_bT[:, h:h + 1],
                              conv_b[h * P:(h + 1) * P].rearrange("(p o) -> p o", o=1)).then_inc(w_in["vec"], 16)
            act.dma_start(bp_col[:, :], bp.rearrange("(p o) -> p o", o=1)).then_inc(w_in["vec"], 16)
            for half, rows in packed:
                act.dma_start(bs_col[rows, :], bs.rearrange("(p o) -> p o", o=1)).then_inc(w_in["vec"], 16)
                act.dma_start(logs[rows, 0:1], A_log.rearrange("(p o) -> p o", o=1)).then_inc(w_in["vec"], 16)
                act.dma_start(logs[rows, 1:2], dt_log.rearrange("(p o) -> p o", o=1)).then_inc(w_in["vec"], 16)
            act.dma_start(Wh_sb[:, :, :], Wh.rearrange("(k p) n -> p k n", p=P)).then_inc(w_in["Wh"], 16)
            act.dma_start(Ws_sb[:, :, :], Ws.rearrange("(k p) n -> p k n", p=P)).then_inc(w_in["Ws"], 16)
            act.dma_start(Wo_bo[0:N, :], Wo).then_inc(w_in["Wo"], 16)
            act.dma_start(Wo_bo[N:N + 1, :], bo.rearrange("(o n) -> o n", o=1)).then_inc(w_in["bo"], 16)
            act.dma_start(b_row[N:N + 1, :], b.rearrange("(o n) -> o n", o=1)).then_inc(w_in["b"], 16)

            act.wait_ge(taps_ps_ready, 1)
            for h in range(HALVES):
                nc.scalar.activation(taps[:, h, :], out_ps[0][:, h * B:(h + 1) * B], ACT.Copy).then_inc(taps_ready, 1)

            def store(c, j):
                k = 2 * c.pair + j
                act.wait_ge(out_ready, c.count(TILES, j + 1))
                act.dma_start(rows_of(out, c, j), out_rows[:, k, :]).then_inc(stored[k], 16)

            def evacuate(c, h):
                if h == 0:
                    act.wait_ge(xt_ps_ready, c.count(1, 1))
                first = HALO + COLS * c.slot
                nc.scalar.activation(xT[:, h, first:first + COLS], xt_ps[:, h * COLS:(h + 1) * COLS],
                                     ACT.Copy).then_inc(xt_ready, 1)

            def history(c, h):
                act.wait_ge(xt_ready, c.count(HALVES, h + 1))
                end = HALO + COLS * RING
                nc.scalar.activation(xT[:, h, 0:HALO], xT[:, h, end - HALO:end], ACT.Copy).then_inc(halo_ready, 1)

            def multiply(c, i):
                h, k = divmod(i, POOL_TAPS)
                at = HALO + COLS * c.slot + (k - TAPS + 1) * B
                src = xT[:, h, at:at + COLS]
                weight = taps[:, h, k:k + 1]
                if k == 0:
                    act.wait_ge(xt_ready, c.count(HALVES, h + 1))
                    if c.slot == 0 and c.at >= RING:
                        act.wait_ge(halo_ready, c.laps(HALVES, -1))
                    if c.at >= 3:
                        act.wait_ge(conv_ready[h], c.count(1, -1))
                    nc.scalar.activation(pool_conv[:, c.pair, h, :], src, ACT.Identity, scale=weight,
                                         bias=conv_bT[:, h:h + 1]).then_inc(pool_base[h], 1)
                    return
                if c.at > 1 or k - 1 + h * (POOL_TAPS - 1) >= 4:
                    act.wait_ge(pool_step, products_before(c, h, k)(-3))
                nc.scalar.activation(products[:, product_slot(c, h, k), :], src, ACT.Copy,
                                     scale=weight).then_inc(product_ready, 1)

            def absolutes(c):
                act.wait_ge(proj_ready, c.count(1, 1))
                if c.at >= 1:
                    act.wait_ge(y_ready, c.count(2, 0))
                for half, rows in packed:
                    nc.scalar.activation(z_abs[rows, :, :], unpacked(proj_ps[0:N, 0:COLS], half), ACT.Abs,
                                         bias=bp_col[0:N, :]).then_inc(abs_ready, 1)

            def exponential(c):
                act.wait_ge(abs_ready, c.count(2, 2))
                nc.scalar.activation(z_exp[:, :, :], z_abs[:, :, :], ACT.Exp, scale=-1.0).then_inc(exp_ready, 1)

            def relus(c):
                for half, rows in packed:
                    nc.scalar.activation(z_relu[rows, :, :], unpacked(proj_ps[0:N, 0:COLS], half), ACT.Relu,
                                         bias=bp_col[0:N, :]).then_inc(relu_ready, 1)

            def inputs(c):
                for half, rows in packed:
                    nc.scalar.activation(u_sb[rows, :, :], unpacked(proj_ps[0:N, COLS:2 * COLS], half),
                                         ACT.Identity, bias=bs_col[0:N, :]).then_inc(u_ready, 1)

            def tanhs(c):
                for half, rows in packed:
                    last = nc.scalar.activation(c_tanh[rows, :, :], unpacked(proj_ps[N:P, 0:COLS], half),
                                                ACT.Tanh, bias=bp_col[N:P, :])
                    last.then_inc(tanh_ready, 1)

            evacuate(Chunk(0, 0), 0)
            evacuate(Chunk(0, 0), 1)
            act.wait_ge(w_in["vec"], 16 * VECTORS)
            nc.scalar.activation(logs_abs[:, :], logs[:, :], ACT.Abs).then_inc(logs_act, 1)
            act.wait_ge(logs_act, 1)
            nc.scalar.activation(logs_exp[:, :], logs_abs[:, :], ACT.Exp, scale=-1.0).then_inc(logs_act, 1)
            nc.scalar.activation(hT[:, RING - 1, :, COLS - B:COLS],
                                 out_ps[0][:, 0:HALVES * B].rearrange("p (h b) -> p h b", h=HALVES),
                                 ACT.Copy).then_inc(h_ready, 1)
            evacuate(Chunk(0, 1), 0)
            evacuate(Chunk(0, 1), 1)
            for i in range(PRODUCTS // 2):
                multiply(Chunk(0, 1), i)
            act.wait_ge(WoT_ps_ready, 1)
            nc.scalar.activation(Wo_boT[:, :, :], out_ps[1][:, 0:HALVES * (N + 1)].rearrange("p (k n) -> p k n", k=HALVES),
                                 ACT.Copy).then_inc(WoT_ready, 1)
            act.wait_ge(Wox_ps_ready, 1)
            nc.scalar.activation(Wox[:, :], out_ps[1][0:N + 1, 0:D], ACT.Copy).then_inc(Wox_copied, 1)
            evacuate(Chunk(0, 2), 0)
            evacuate(Chunk(0, 2), 1)
            for i in range(PRODUCTS // 2, PRODUCTS):
                multiply(Chunk(0, 1), i)
            absolutes(Chunk(0, 0))
            exponential(Chunk(0, 0))
            relus(Chunk(0, 0))
            inputs(Chunk(0, 0))
            tanhs(Chunk(0, 0))
            for i in range(STEPS - 3):
                multiply(Chunk(0, 2), i)

            def window(c, w):
                for s in range(STEPS):
                    act.wait_ge(mm_ready, c.count(STEPS, s + 1))
                    cols = slice(s * B, (s + 1) * B)
                    nc.scalar.activation(hT[:, c.slot, :, cols], rec_ps[c.pair][:, :, cols], ACT.Tanh).then_inc(h_ready, 1)
                    if exists(w, 1):
                        n = c + 1
                        if s == 4:
                            absolutes(n)
                        if s == 5:
                            exponential(n)
                        if s == 6:
                            inputs(n)
                        if s == 7:
                            relus(n)
                        if s == 8:
                            tanhs(n)
                    if exists(w, 2) and s < 3:
                        multiply(c + 2, STEPS - 3 + s)
                    if exists(w, 3):
                        if s in (2, 3):
                            evacuate(c + 3, s - 2)
                        if s >= 3:
                            multiply(c + 3, s - 3)
                        if (c + 3).slot == RING - 1 and s in (12, 13):
                            history(c + 3, s - 12)
                    if exists(w, -1) and s == 9:
                        store(c + -1, 1)
                    if exists(w, -1) and s == 1:
                        store(c + -1, 0)

            windows(act, window)
            store(Chunk(0, CHUNKS - 1), 0)
            store(Chunk(0, CHUNKS - 1), 1)

        @block.tensor
        def _(pe):
            def transposes(c, j):
                if j == 0:
                    pe.wait_ge(rows_in[c.slot], c.laps(16 * TILES))
                    if c.at >= 1:
                        pe.wait_ge(xt_ready, c.count(HALVES, 0))
                for h in range(HALVES):
                    last = nc.tensor.transpose(xt_ps[:, h * COLS + j * P:h * COLS + (j + 1) * P],
                                               x_rows[:, c.slot, j, h * P:(h + 1) * P], ident[:, :])
                if j == TILES - 1:
                    last.then_inc(xt_ps_ready, 1)

            def xT_of(c, h):
                first = HALO + COLS * c.slot
                return xT[:, h, first:first + COLS]

            def inputs(c, k):
                if k == 0 and c.at >= 1:
                    pe.wait_ge(tanh_ready, c.count(2, 0))
                pe.wait_ge(xt_ready, c.count(HALVES, k + 1))
                nc.tensor.matmul(proj_ps[0:N, COLS:2 * COLS], Ws_sb[:, k, :], xT_of(c, k),
                                 start=k == 0, stop=k == HALVES - 1)

            def project(c, k):
                pe.wait_ge(conv_ready[k], c.count(1, 1))
                last = nc.tensor.matmul(proj_ps[:, 0:COLS], Wp_sb[:, k, :], conv[:, c.pair, k, :],
                                        start=k == 0, stop=k == HALVES - 1)
                if k == HALVES - 1:
                    last.then_inc(proj_ready, 1)

            def drive_x(c, m, k):
                nc.tensor.matmul(rec_ps[c.pair][:, m, 0:COLS], Wx_sb[:, k, m * P:(m + 1) * P], xT_of(c, k),
                                 start=k == 0, stop=False, skip_group_check=True)

            def drive_y(c, m):
                if m == 0:
                    pe.wait_ge(y_ready, c.count(2, 2))
                nc.tensor.matmul(rec_ps[c.pair][:, m, 0:COLS], Wox[:, m * P:(m + 1) * P], yT[:, c.slot, :],
                                 start=False, stop=False, skip_group_check=True)

            def out_y(c, j):
                nc.tensor.matmul(out_ps[j][:, 0:D], yT[:, c.slot, j * P:(j + 1) * P], Wo_bo[:, :],
                                 start=True, stop=False, skip_group_check=True)

            def out_h(c, j):
                pe.wait_ge(h_ready, c.count(STEPS, (j + 1) * TILE_T + 1))
                for m in range(HALVES):
                    last = nc.tensor.matmul(out_ps[j][:, m * P:(m + 1) * P],
                                            hT[:, c.slot, m, j * P:(j + 1) * P], ident[:, :],
                                            is_transpose=True,
                                            start=False, stop=True, skip_group_check=True)
                last.then_inc(out_ps_ready, 1)

            def twice(bank):
                return bank.rearrange("p (d n) -> p d n", d=2)

            def step(c, s):
                before = c if s else c + -1
                col = (s - 1) % STEPS * B
                h = [hT[:, before.slot, k, col:col + B] for k in range(HALVES)]
                parts = [[v.bitcast(BF16)[:, 1::2] for v in h],
                         [h_rest[:, s % 2, k, :].bitcast(BF16)[:, 1::2] for k in range(HALVES)],
                         [h_last[:, s % 2, k, :] for k in range(HALVES)]]
                ready = [h_ready, rest_ready, last_ready]
                for p in range(3):
                    pe.wait_ge(ready[p], c.count(STEPS, s + 1))
                    for m in range(HALVES):
                        for k in range(HALVES):
                            for a in range(3 - p):
                                last = nc.tensor.matmul(twice(rec_ps[c.pair][:, m, :])[:, :, s * B:(s + 1) * B],
                                                        Wh_parts[:, a, k, m * P:(m + 1) * P],
                                                        parts[p][k].unsqueeze(1).broadcast_to([P, 2, B]),
                                                        start=False, stop=p == 2 and k == 1, skip_group_check=True)
                last.then_inc(mm_ready, 1)

            pe.wait_ge(ident_ready, 2)
            pe.wait_ge(w_in["cond"], 16)
            for h in range(HALVES):
                last = nc.tensor.transpose(out_ps[0][:, h * B:(h + 1) * B], cond_sb[:, h * P:(h + 1) * P], ident[0:B, 0:B])
            last.then_inc(taps_ps_ready, 1)
            transposes(Chunk(0, 0), 0)
            transposes(Chunk(0, 0), 1)
            pe.wait_ge(w_in["Wo"], 16)
            pe.wait_ge(w_in["bo"], 16)
            for h in range(HALVES):
                last = nc.tensor.transpose(out_ps[1][:, h * (N + 1):(h + 1) * (N + 1)], Wo_bo[:, h * P:(h + 1) * P],
                                           ident[0:N + 1, 0:N + 1])
            last.then_inc(WoT_ps_ready, 1)
            transposes(Chunk(0, 1), 0)
            transposes(Chunk(0, 1), 1)
            pe.wait_ge(w_in["Wx"], 16)
            pe.wait_ge(WoT_ready, 1)
            for k in range(HALVES):
                last = nc.tensor.matmul(out_ps[1][0:N + 1, 0:D], Wo_boT[:, k, :], Wx_sb[:, k, :],
                                        start=k == 0, stop=k == HALVES - 1)
            last.then_inc(Wox_ps_ready, 1)
            transposes(Chunk(0, 2), 0)
            transposes(Chunk(0, 2), 1)
            pe.wait_ge(w_in["Ws"], 16)
            for k in range(HALVES):
                inputs(Chunk(0, 0), k)
            for m in range(HALVES):
                for k in range(HALVES):
                    drive_x(Chunk(0, 0), m, k)
            pe.wait_ge(w_in["Wp"], 16)
            for k in range(HALVES):
                project(Chunk(0, 0), k)
            pe.wait_ge(Wox_ready, 1)
            pe.wait_ge(cleared, 2)
            for m in range(HALVES):
                drive_y(Chunk(0, 0), m)
            for k in range(HALVES):
                inputs(Chunk(0, 1), k)
            pe.wait_ge(split, SPLITS)

            def window(c, w):
                for s in range(STEPS):
                    step(c, s)
                    if exists(w, 3) and s in (0, 1):
                        transposes(c + 3, s)
                    if exists(w, 1):
                        n = c + 1
                        if s in (2, 3):
                            project(n, s - 2)
                        elif 6 <= s < 10:
                            drive_x(n, (s - 6) // 2, s % 2)
                        elif s >= 14:
                            drive_y(n, s - 14)
                    if exists(w, 2) and s in (10, 11):
                        inputs(c + 2, s - 10)
                    if exists(w, -1):
                        if s == 4:
                            out_y(c + -1, 1)
                        if s == 5:
                            out_h(c + -1, 1)
                    if s == 12:
                        out_y(c, 0)
                    if s == 13:
                        out_h(c, 0)

            windows(pe, window)
            out_y(Chunk(0, CHUNKS - 1), 1)
            out_h(Chunk(0, CHUNKS - 1), 1)

        @block.vector
        def _(dve):
            const_count = [0]

            def const(instruction):
                instruction.then_inc(consts, 1)
                const_count[0] += 1
                dve.wait_ge(consts, const_count[0])

            for k in range(RING):
                dve.sem_inc(stored[k], 16)
            nc.vector.memset(xT[:, :, 0:HALO], 0.0).then_inc(cleared, 1)
            nc.vector.memset(yT[N:N + 1, :, :], 1.0).then_inc(cleared, 1)

            def taps_of(c, h, k, first_tap):
                acc = conv[:, c.pair, h, :]
                at = HALO + COLS * c.slot + (k - TAPS + 1) * B
                src = xT[:, h, at:at + COLS]
                weight = taps[:, h, k:k + 1]
                if k == first_tap:
                    if c.slot == 0 and c.at >= RING:
                        dve.wait_ge(halo_ready, c.laps(HALVES, -1))
                    if c.at == 0 and isinstance(c.lap, int):
                        dve.wait_ge(xt_ready, c.count(HALVES, h + 1))
                        ins = nc.vector.tensor_scalar(acc, src, weight, conv_bT[:, h:h + 1], ALU.mult, ALU.add)
                    else:
                        dve.wait_ge(pool_step, products_before(c, h, POOL_TAPS - 1)(1))
                        ins = nc.vector.scalar_tensor_tensor(out=acc, in0=src, scalar=weight,
                                                             in1=pool_conv[:, c.pair, h, :], op0=ALU.mult, op1=ALU.add)
                else:
                    dve.wait_ge(conv_step[h], c.count(TAPS - POOL_TAPS - 1,
                                                      k - first_tap + (POOL_TAPS if c.at >= 1 or not isinstance(c.lap, int) else 0)))
                    ins = nc.vector.scalar_tensor_tensor(out=acc, in0=src, scalar=weight, in1=acc,
                                                         op0=ALU.mult, op1=ALU.add)
                ins.then_inc(conv_ready[h] if k == TAPS - 1 else conv_step[h], 1)

            def log1p(acc, e, link):
                link(nc.vector.tensor_scalar(acc, e, LOG1P[-1], None, ALU.mult))
                for coefficient in LOG1P[-2::-1]:
                    link(nc.vector.scalar_tensor_tensor(out=acc, in0=acc, scalar=coefficient, in1=e,
                                                        op0=ALU.add, op1=ALU.mult))

            def tail(c, i):
                def before():
                    dve.wait_ge(tail_step, c.count(CHAIN, i))
                n = len(LOG1P)
                s_now, s_old = state[:, c.pair, :, :], state[:, 1 - c.pair, :, :]
                if i == 0:
                    dve.wait_ge(exp_ready, c.count(1, 1))
                    nc.vector.tensor_scalar(drive[:, :, :], z_exp[:, :, :], LOG1P[-1], None,
                                            ALU.mult).then_inc(tail_step, 1)
                elif i < n:
                    before()
                    nc.vector.scalar_tensor_tensor(out=drive[:, :, :], in0=drive[:, :, :], scalar=LOG1P[n - 1 - i],
                                                   in1=z_exp[:, :, :], op0=ALU.add, op1=ALU.mult).then_inc(tail_step, 1)
                elif i == n:
                    before()
                    dve.wait_ge(relu_ready, c.count(2, 2))
                    nc.vector.tensor_tensor(drive[:, :, :], drive[:, :, :], z_relu[:, :, :], ALU.add).then_inc(tail_step, 1)
                elif i == n + 1:
                    before()
                    dve.wait_ge(u_ready, c.count(2, 2))
                    nc.vector.tensor_tensor(drive[:, :, :], drive[:, :, :], u_sb[:, :, :], ALU.mult).then_inc(tail_step, 1)
                elif i == n + 2:
                    before()
                    nc.vector.scalar_tensor_tensor(out=drive[:, :, 0], in0=s_old[:, :, STEPS - 1], scalar=decay[:, :],
                                                   in1=drive[:, :, 0], op0=ALU.mult, op1=ALU.add).then_inc(tail_step, 1)
                elif i == n + 3:
                    before()
                    nc.vector.tensor_tensor_scan(s_now.rearrange("p b t -> p (b t)"),
                                                 decays[:, :, :].rearrange("p b t -> p (b t)"),
                                                 drive[:, :, :].rearrange("p b t -> p (b t)"),
                                                 0.0, ALU.mult, ALU.add).then_inc(tail_step, 1)
                else:
                    half = i - n - 4
                    rows = packed[half][1]
                    if half == 0:
                        dve.wait_ge(tail_step, c.count(CHAIN, CHAIN))
                        dve.wait_ge(tanh_ready, c.count(2, 2))
                    nc.vector.scalar_tensor_tensor(out=unpacked(yT[0:N, c.slot, :], half), in0=c_tanh[rows, :, :],
                                                   scalar=logs_sp[rows, 1:2], in1=s_now[rows, :, :],
                                                   op0=ALU.mult, op1=ALU.mult).then_inc(y_ready, 1)

            TAIL = CHAIN + 2

            def state_parts(g, h, q):
                dve.wait_ge(h_ready, g)
                rest = h_rest[:, q, :, :]
                nc.vector.tensor_tensor(rest, h, h.bitcast(BF16)[:, :, 1::2], ALU.subtract).then_inc(rest_ready, 1)
                dve.wait_ge(rest_ready, g)
                nc.vector.tensor_tensor(h_last[:, q, :, :], rest, rest.bitcast(BF16)[:, :, 1::2],
                                        ALU.subtract).then_inc(last_ready, 1)

            def add_x(c, j):
                k = 2 * c.pair + j
                dve.wait_ge(out_ps_ready, c.count(TILES, j + 1))
                if j == 0:
                    dve.wait_ge(again_in[c.slot], c.laps(16 * TILES))
                dve.wait_ge(stored[k], stores_before(c))
                nc.vector.tensor_tensor(out_rows[:, k, :], out_ps[j][:, 0:D], x_again[:, c.slot, j, :],
                                        ALU.add).then_inc(out_ready, 1)

            dve.wait_ge(taps_ready, HALVES)
            dve.wait_ge(w_in["vec"], 16 * VECTORS)
            dve.wait_ge(cleared, 2)
            for k in range(TAPS):
                for h in range(HALVES):
                    taps_of(Chunk(0, 0), h, k, 0)

            dve.wait_ge(w_in["Wh"], 16)
            done = 0
            left = Wh_sb
            for a in range(3):
                nc.vector.tensor_copy(Wh_parts[:, a, :, :], left[:, :, :]).then_inc(split, 1)
                done += 1
                dve.wait_ge(split, done)
                if a < 2:
                    nc.vector.tensor_tensor(Wh_rest[:, :, :], left[:, :, :], Wh_parts[:, a, :, :],
                                            ALU.subtract).then_inc(split, 1)
                    done += 1
                    dve.wait_ge(split, done)
                    left = Wh_rest
            assert done == SPLITS

            dve.wait_ge(logs_act, 2)
            log1p(logs_sp[:, :], logs_exp[:, :], const)
            const(nc.vector.scalar_tensor_tensor(out=logs_sp[:, :], in0=logs[:, :], scalar=0.0, in1=logs_sp[:, :],
                                                 op0=ALU.max, op1=ALU.add))
            const(nc.vector.tensor_tensor(dt_A[:, :], logs_sp[:, 0:1], logs_sp[:, 1:2], ALU.mult))
            const(nc.vector.tensor_scalar(decay[:, :], dt_A[:, :], -1.0, 1.0, ALU.mult, ALU.add))
            const(nc.vector.memset(decays[:, :, :], 1.0))
            const(nc.vector.memset(decays[:, :, 0], 0.0))
            const(nc.vector.tensor_scalar(decays[:, :, :], decays[:, :, :], decay[:, :], None, ALU.mult))
            const(nc.vector.memset(state[:, 1, :, :], 0.0))

            dve.wait_ge(Wox_copied, 1)
            dve.wait_ge(w_in["b"], 16)
            nc.vector.tensor_tensor(Wox[N:N + 1, :], Wox[N:N + 1, :], b_row[N:N + 1, :], ALU.add).then_inc(Wox_ready, 1)
            for i in range(TAIL):
                tail(Chunk(0, 0), i)
            state_parts(1, hT[:, RING - 1, :, COLS - B:COLS], 0)
            for k in range(POOL_TAPS, TAPS):
                for h in range(HALVES):
                    taps_of(Chunk(0, 1), h, k, POOL_TAPS)

            own = [(h, k) for h in range(HALVES) for k in range(POOL_TAPS, TAPS)]

            def window(c, w):
                for s in range(STEPS):
                    state_parts(c.count(STEPS, s + 2), hT[:, c.slot, :, s * B:(s + 1) * B], (s + 1) % 2)
                    if exists(w, 2):
                        first = 2 * s if s < 6 else 2 * (s - 8) if s >= 14 else None
                        if first is not None:
                            for h, k in own[first:first + 2]:
                                taps_of(c + 2, h, k, POOL_TAPS)
                    if exists(w, 1) and 6 <= s < 14:
                        for i in range(2 * (s - 6), min(2 * (s - 6) + 2, TAIL)):
                            tail(c + 1, i)
                    if exists(w, -1) and s == 6:
                        add_x(c + -1, 1)
                    if s == 14:
                        add_x(c, 0)

            windows(dve, window)
            add_x(Chunk(0, CHUNKS - 1), 1)


def kernel(x, cond_1024, L0_cond_conv_b, L0_cond_Wp, L0_cond_bp, L0_cond_Ws, L0_cond_bs, L0_cond_A_log,
           L0_cond_dt_log, L0_cond_Wo, L0_cond_bo, L1_cond_Wx, L1_cond_Wh, L1_cond_b):
    import numpy as np
    import concourse.bacc as bacc
    from concourse.bass_utils import run_bass_kernel_spmd

    given = dict(x=x, cond=cond_1024, conv_b=L0_cond_conv_b, Wp=L0_cond_Wp, bp=L0_cond_bp, Ws=L0_cond_Ws,
                 bs=L0_cond_bs, A_log=L0_cond_A_log, dt_log=L0_cond_dt_log, Wo=L0_cond_Wo, bo=L0_cond_bo,
                 Wx=L1_cond_Wx, Wh=L1_cond_Wh, b=L1_cond_b)
    nc = bacc.Bacc("TRN2", target_bir_lowering=False, num_devices=1)
    arrays, args = {}, {}
    for name, a in given.items():
        a = np.ascontiguousarray(a)
        arrays[f"in_{name}"] = a
        args[name] = nc.dram_tensor(f"in_{name}", a.shape, mybir.dt.from_np(a.dtype), kind="ExternalInput").ap()
    args["out"] = nc.dram_tensor("out_dram", x.shape, FP32, kind="ExternalOutput").ap()
    build(nc, **args)
    r = run_bass_kernel_spmd(nc, [arrays], core_ids=[0])
    return r.results[0]["out_dram"]
```

```python
import concourse.bass as bass
from concourse import mybir
from contextlib import ExitStack

FP32 = mybir.dt.float32
BF16 = mybir.dt.bfloat16
ACT = mybir.ActivationFunctionType
ALU = mybir.AluOpType

SQUARE_SCALE = 0.5188665390014648
LOG1P = [(-0.042396362870931625, 0.8761447668075562), (-0.7386612892150879, 0.7267640233039856),
         (-1.2038626670837402, 0.11630015820264816), (0.5237411260604858, 0.29748833179473877)]


class Chunk:

    def __init__(self, lap, at):
        self.lap, self.at = lap, at

    def __add__(self, d):
        return Chunk(self.lap, self.at + d)

    def count(self, per_chunk, plus):
        v = per_chunk * self.at + plus
        return v if isinstance(self.lap, int) else self.lap * (4 * per_chunk) + v

    def laps(self, per_lap, plus=0):
        v = per_lap * (self.at // 4 + 1 + plus)
        return v if isinstance(self.lap, int) else self.lap * per_lap + v

    @property
    def slot(self):
        return self.at % 4

    @property
    def pair(self):
        return self.at % 2


def build(nc, x, cond, conv_b, Wp, bp, Ws, bs, A_log, dt_log, Wo, bo, Wx, Wh, b, out):
    B, L, D = x.shape
    N = Ws.shape[1]
    TAPS = B
    P = 128
    HALVES = D // P
    STEPS = 16
    COLS = STEPS * B
    CHUNKS = L // STEPS
    RING = 4
    HALO = (TAPS - 1) * B
    TILE_T = P // B
    TILES = COLS // P
    BH = B // 2
    POOL_TAPS = 8
    PE_TAPS = {1: (6, 4), 2: (3, 3)}
    FIRST_POOL_TAPS = {1: (4, 4), 2: (5, 5)}
    PRODUCT_BUFFERS = 4
    FIRST_LOOPED, LAPS = 1, 3
    assert CHUNKS == FIRST_LOOPED + RING * LAPS + 3 and 2 * N == P and TILES == 2 and HALVES == 2

    ctx = ExitStack()
    with ctx:
        def sb(name, shape, dt=FP32):
            return ctx.enter_context(nc.sbuf_tensor(name, shape, dt))

        def sem(name):
            return ctx.enter_context(nc.semaphore(name))

        most_diagonals = max(max(n) for n in PE_TAPS.values())

        Wp_sb = sb("Wp_sb", [P, HALVES, 2 * N])
        Ws_sb = sb("Ws_sb", [P, HALVES, N])
        Wx_sb = sb("Wx_sb", [P, HALVES, D])
        Wh_sb = sb("Wh_sb", [P, HALVES, D])
        Wh_rest = sb("Wh_rest", [P, HALVES, D])
        Wh_parts = sb("Wh_parts", [P, 3, HALVES, D], BF16)
        diagonals = sb("diagonals", [P, HALVES, most_diagonals, P])
        Wo_bo = sb("Wo_bo", [N + 1, D])
        Wo_boT = sb("Wo_boT", [P, HALVES, N + 1])
        Wox = sb("Wox", [N + 1, D])
        b_row = sb("b_row", [N + 1, D])
        cond_rows = sb("cond_rows", [B + 1, D])
        bp_row = sb("bp_row", [1, 2 * N])
        n_rows = sb("n_rows", [3, N])
        columns = sb("columns", [P, HALVES * (TAPS + 1) + 4])
        taps = columns[:, 0:HALVES * (TAPS + 1)].rearrange("p (h k) -> p h k", h=HALVES)
        conv_bT = taps[:, :, TAPS]
        after = HALVES * (TAPS + 1)
        bp_col = columns[:, after:after + 1]
        bs_col = columns[:, after + 1:after + 2]
        logs = columns[:, after + 2:after + 4]
        warm = sb("warm", [P, len(LOG1P)])
        logs_abs = sb("logs_abs", [P, 2])
        logs_exp = sb("logs_exp", [P, 2])
        logs_squares = sb("logs_squares", [P, len(LOG1P), 2])
        logs_sp = sb("logs_sp", [P, 2])
        dt_A = sb("dt_A", [P, 1])
        decay = sb("decay", [P, 1])
        decays = sb("decays", [P, BH, STEPS])
        ident = sb("ident", [P, P])
        x_rows = sb("x_rows", [P, RING, TILES, D])
        x_again = sb("x_again", [P, RING, TILES, D])
        xT = sb("xT", [P, HALVES, HALO + RING * COLS])
        products = sb("products", [P, PRODUCT_BUFFERS, COLS])
        pool_conv = sb("pool_conv", [P, 2, HALVES, COLS])
        conv = sb("conv", [P, 2, HALVES, COLS])
        z_abs = sb("z_abs", [P, BH, STEPS])
        z_exp = sb("z_exp", [P, BH, STEPS])
        z_squares = sb("z_squares", [P, len(LOG1P), BH, STEPS])
        z_relu = sb("z_relu", [P, BH, STEPS])
        shifts = sb("shifts", [P, len(LOG1P)])
        u_sb = sb("u_sb", [P, BH, STEPS])
        c_tanh = sb("c_tanh", [P, BH, STEPS])
        drive = sb("drive", [P, BH, STEPS])
        state = sb("state", [P, 2, BH, STEPS])
        yT = sb("yT", [N + 1, RING, COLS])
        hT = sb("hT", [P, RING, HALVES, COLS])
        h_rest = sb("h_rest", [P, 2, HALVES, B])
        h_last = sb("h_last", [P, 2, HALVES, B], BF16)
        out_rows = sb("out_rows", [P, RING, D])

        BANK = 512
        psum = ctx.enter_context(nc.psum_tensor("psum", [P, 8 * BANK], FP32))
        rec_ps = [psum[:, 2 * q * BANK:2 * (q + 1) * BANK].rearrange("p (m n) -> p m n", m=HALVES)
                  for q in range(2)]
        xt_ps, proj_ps, *out_ps = [psum[:, q * BANK:(q + 1) * BANK] for q in range(4, 8)]

        w_in = {n: sem("in_" + n) for n in ("Wp", "Ws", "Wx", "Wh", "Wo", "bo", "b", "cond", "conv_b", "vectors")}
        rows_in = [sem(f"rows_in{r}") for r in range(RING)]
        again_in = [sem(f"again_in{r}") for r in range(RING)]
        cleared = sem("cleared")
        ident_ready = sem("ident_ready")
        taps_ps_ready = sem("taps_ps_ready")
        vectors_ps_ready = sem("vectors_ps_ready")
        vectors_ready = sem("vectors_ready")
        shifts_ready = sem("shifts_ready")
        diagonals_ready = sem("diagonals_ready")
        diagonal_sums = sem("diagonal_sums")
        taps_ready = sem("taps_ready")
        WoT_ps_ready = sem("WoT_ps_ready")
        WoT_ready = sem("WoT_ready")
        Wox_ps_ready = sem("Wox_ps_ready")
        Wox_copied = sem("Wox_copied")
        Wox_ready = sem("Wox_ready")
        split = sem("split")
        consts = sem("consts")
        logs_act = sem("logs_act")
        xt_ps_ready = sem("xt_ps_ready")
        xt_ready = sem("xt_ready")
        halo_ready = sem("halo_ready")
        pool_step = sem("pool_step")
        product_ready = sem("product_ready")
        pool_base = [sem(f"pool_base{h}") for h in range(HALVES)]
        conv_step = [sem(f"conv_step{h}") for h in range(HALVES)]
        conv_ready = [sem(f"conv_ready{h}") for h in range(HALVES)]
        proj_ready = sem("proj_ready")
        abs_ready = sem("abs_ready")
        exp_ready = sem("exp_ready")
        squares_ready = sem("squares_ready")
        relu_ready = sem("relu_ready")
        u_ready = sem("u_ready")
        tanh_ready = sem("tanh_ready")
        tail_step = sem("tail_step")
        y_ready = sem("y_ready")
        mm_ready = sem("mm_ready")
        h_ready = sem("h_ready")
        rest_ready = sem("rest_ready")
        last_ready = sem("last_ready")
        out_ps_ready = sem("out_ps_ready")
        out_ready = sem("out_ready")
        stored = [sem(f"stored{r}") for r in range(RING)]

        block = ctx.enter_context(nc.Block())
        SPLITS = 4
        CLEARED = 4
        FIRST_AT = dict(project=3, transposes=0, evacuate=2, absolutes=5, exponential=6, squares={7: (0, 1), 8: (2, 3)},
                        relus=9, inputs=10, tanhs=11,
                        tail={7: (0,), 8: (1,), 9: (2,), 10: (3, 4), 11: (5, 6), 12: (7, 8), 13: (9,)})
        USUAL_AT = dict(project=0, transposes=4, evacuate=6, absolutes=2, exponential=3,
                        squares={4: (0,), 5: (1,), 6: (2,), 7: (3,)}, relus=8, inputs=9, tanhs=10,
                        tail={5: (0,), 6: (1,), 7: (2,), 8: (3,), 9: (4,), 10: (5,), 11: (6, 7), 12: (8, 9)})
        CARRIED = 7
        CHAIN = len(LOG1P) + 4

        def windows(eng, window):
            for w in range(FIRST_LOOPED):
                window(Chunk(0, w), w)
            with eng.Fori(0, LAPS) as lap:
                for w in range(RING):
                    window(Chunk(lap, FIRST_LOOPED + w), None)
            for w in range(CHUNKS - 3, CHUNKS):
                window(Chunk(0, w), w)

        PRODUCTS = HALVES * POOL_TAPS
        SUMS = HALVES * (POOL_TAPS - 1)

        FIRST_SUMS = sum(FIRST_POOL_TAPS[1]) + sum(FIRST_POOL_TAPS[2])

        def is_early(c):
            return isinstance(c.lap, int) and c.at in PE_TAPS

        def sums_before(c, h, k):
            if is_early(c):
                first = sum(FIRST_POOL_TAPS[1]) * (c.at - 1) + sum(FIRST_POOL_TAPS[c.at][:h]) + k - PE_TAPS[c.at][h]
                return lambda plus: first + plus
            return lambda plus: (c + -3).count(SUMS, FIRST_SUMS + h * (POOL_TAPS - 1) + k - 1 + plus)

        def product_slot(c, h, k):
            return sums_before(Chunk(0, c.at), h, k)(0) % PRODUCT_BUFFERS

        def dve_first(c, h):
            return PE_TAPS[c.at][h] + FIRST_POOL_TAPS[c.at][h] if is_early(c) else POOL_TAPS

        def dve_taps_before(c, h, k):
            steps = [TAPS - 1] + [TAPS - dve_first(Chunk(0, n), h) - 1 for n in PE_TAPS]
            if is_early(c):
                return sum(steps[:c.at]) + k - dve_first(c, h)
            return (c + -3).count(TAPS - POOL_TAPS - 1, sum(steps) + k - POOL_TAPS)

        def stores_before(c):
            v = 16 * (c.at // 2 + 1)
            return v if isinstance(c.lap, int) else c.lap * (16 * RING // 2) + v

        def exists(w, ahead):
            return w is None or 0 <= w + ahead < CHUNKS

        def rows_of(t, c, j):
            first = c.count(STEPS, TILE_T * j)
            return t[:, bass.ds(first, TILE_T), :].rearrange("b t d -> t b d")

        @block.sync
        def _(sp):
            def load(dst, c, done):
                for j in range(TILES):
                    sp.dma_start(dst[:, c.slot, j, :], rows_of(x, c, j)).then_inc(done[c.slot], 16)

            sp.dma_start(cond_rows[0:B, :], cond).then_inc(w_in["cond"], 16)
            load(x_rows, Chunk(0, 0), rows_in)
            load(x_rows, Chunk(0, 1), rows_in)
            sp.dma_start(Wh_sb[:, :, :], Wh.rearrange("(k p) n -> p k n", p=P)).then_inc(w_in["Wh"], 16)
            sp.dma_start(Ws_sb[:, :, :], Ws.rearrange("(k p) n -> p k n", p=P)).then_inc(w_in["Ws"], 16)
            sp.dma_start(Wo_bo[0:N, :], Wo).then_inc(w_in["Wo"], 16)
            sp.dma_start(Wx_sb[:, :, :], Wx.rearrange("(k p) n -> p k n", p=P)).then_inc(w_in["Wx"], 16)
            load(x_rows, Chunk(0, 2), rows_in)
            sp.dma_start(Wp_sb[:, :, :], Wp.rearrange("(k p) n -> p k n", p=P)).then_inc(w_in["Wp"], 16)

            def load_chunk(c):
                sp.wait_ge(xt_ps_ready, c.count(1, -RING + 1))
                load(x_rows, c, rows_in)
                sp.wait_ge(out_ready, c.count(TILES, -(RING - 1) * TILES))
                load(x_again, c, again_in)

            for n in range(RING):
                if n == RING - 1:
                    load(x_rows, Chunk(0, n), rows_in)
                load(x_again, Chunk(0, n), again_in)
            with sp.Fori(0, CHUNKS // RING - 1) as lap:
                for n in range(RING):
                    load_chunk(Chunk(lap, RING + n))
            for k in range(RING):
                sp.wait_ge(stored[k], 16 * (CHUNKS // 2 + 1))

        @block.gpsimd
        def _(pool):
            pool.memset(ident[:, :], 0.0).then_inc(ident_ready, 1)
            for i, (shift, _) in enumerate(LOG1P):
                pool.memset(shifts[:, i:i + 1], shift).then_inc(shifts_ready, 1)
            pool.wait_ge(ident_ready, 1)
            pool.affine_select(out=ident[:, :], in_=ident[:, :], compare_op=ALU.not_equal, fill=1.0,
                               base=0, pattern=[[-1, P]], channel_multiplier=1).then_inc(ident_ready, 1)
            pool.dma_start(bp_row[:, :], bp.rearrange("(o n) -> o n", o=1)).then_inc(w_in["vectors"], 16)
            for row, v in enumerate((bs, A_log, dt_log)):
                pool.dma_start(n_rows[row:row + 1, :], v.rearrange("(o n) -> o n", o=1)).then_inc(w_in["vectors"], 16)
            pool.dma_start(Wo_bo[N:N + 1, :], bo.rearrange("(o n) -> o n", o=1)).then_inc(w_in["bo"], 16)

            def add_taps(c, h, k, first=1):
                p = sums_before(c, h, k)
                pool.wait_ge(product_ready, p(1))
                if k > first:
                    pool.wait_ge(pool_step, p(0))
                else:
                    pool.wait_ge(pool_base[h], c.count(1, 0))
                acc = pool_conv[:, c.pair, h, :]
                ins = pool.tensor_tensor(acc, acc, products[:, product_slot(c, h, k), :], ALU.add)
                ins.then_inc(pool_step, 1)

            pool.wait_ge(taps_ready, 1)
            pool.wait_ge(ident_ready, 2)
            for h in range(HALVES):
                n = max(PE_TAPS[c][h] for c in PE_TAPS)
                pool.tensor_tensor(diagonals[:, h, 0:n, :], ident[:, :].unsqueeze(1).broadcast_to([P, n, P]),
                                   taps[:, h, 0:n].unsqueeze(2).broadcast_to([P, n, P]),
                                   ALU.mult).then_inc(diagonals_ready, 1)

            pool.dma_start(b_row[N:N + 1, :], b.rearrange("(o n) -> o n", o=1)).then_inc(w_in["b"], 16)

            pool.wait_ge(split, 1)
            pool.tensor_tensor(Wh_rest[:, :, :], Wh_sb[:, :, :], Wh_parts[:, 0, :, :], ALU.subtract).then_inc(split, 1)
            pool.wait_ge(split, 3)
            pool.tensor_tensor(Wh_parts[:, 2, :, :], Wh_rest[:, :, :], Wh_parts[:, 1, :, :], ALU.subtract).then_inc(split, 1)
            for n in PE_TAPS:
                for h in range(HALVES):
                    for k in range(FIRST_POOL_TAPS[n][h]):
                        add_taps(Chunk(0, n), h, PE_TAPS[n][h] + k, PE_TAPS[n][h])

            def window(c, w):
                if exists(w, 3):
                    for h in range(HALVES):
                        for k in range(1, POOL_TAPS):
                            add_taps(c + 3, h, k)

            windows(pool, window)

        packed = [(0, slice(0, N)), (1, slice(N, P))]

        def unpacked(ap, half):
            return ap.rearrange("p (t b) -> p b t", b=B)[:, half * BH:(half + 1) * BH, :]

        @block.scalar
        def _(act):
            act.dma_start(cond_rows[B:B + 1, :], conv_b.rearrange("(o n) -> o n", o=1)).then_inc(w_in["conv_b"], 16)
            act.wait_ge(shifts_ready, len(LOG1P))
            nc.scalar.activation(warm[:, :], shifts[:, :], ACT.Exp)
            act.wait_ge(taps_ps_ready, 1)
            nc.scalar.activation(columns[:, 0:after], out_ps[0][:, 0:after], ACT.Copy).then_inc(taps_ready, 1)

            def store(c, j):
                k = 2 * c.pair + j
                act.wait_ge(out_ready, c.count(TILES, j + 1))
                act.dma_start(rows_of(out, c, j), out_rows[:, k, :]).then_inc(stored[k], 16)

            def evacuate(c, h):
                if h == 0:
                    act.wait_ge(xt_ps_ready, c.count(1, 1))
                first = HALO + COLS * c.slot
                nc.scalar.activation(xT[:, h, first:first + COLS], xt_ps[:, h * COLS:(h + 1) * COLS],
                                     ACT.Copy).then_inc(xt_ready, 1)

            def history(c, h):
                act.wait_ge(xt_ready, c.count(HALVES, h + 1))
                end = HALO + COLS * RING
                nc.scalar.activation(xT[:, h, 0:HALO], xT[:, h, end - HALO:end], ACT.Copy).then_inc(halo_ready, 1)

            def from_diagonals(n, h):
                act.wait_ge(diagonal_sums, (n - 1) * HALVES + h + 1)
                nc.scalar.activation(pool_conv[:, n % 2, h, :], rec_ps[1][:, h, (n - 1) * COLS:n * COLS], ACT.Identity,
                                     bias=conv_bT[:, h:h + 1]).then_inc(pool_base[h], 1)

            def multiply(c, h, k):
                at = HALO + COLS * c.slot + (k - TAPS + 1) * B
                src = xT[:, h, at:at + COLS]
                weight = taps[:, h, k:k + 1]
                if k == 0:
                    act.wait_ge(xt_ready, c.count(HALVES, h + 1))
                    if c.slot == 0 and c.at >= RING:
                        act.wait_ge(halo_ready, c.laps(HALVES, -1))
                    act.wait_ge(conv_ready[h], c.count(1, -1))
                    nc.scalar.activation(pool_conv[:, c.pair, h, :], src, ACT.Identity, scale=weight,
                                         bias=conv_bT[:, h:h + 1]).then_inc(pool_base[h], 1)
                    return
                if is_early(c) and k == PE_TAPS[c.at][h]:
                    act.wait_ge(xt_ready, c.count(HALVES, h + 1))
                if not (c.at == 1 and is_early(c) and sums_before(c, h, k)(0) < PRODUCT_BUFFERS):
                    act.wait_ge(pool_step, sums_before(c, h, k)(1 - PRODUCT_BUFFERS))
                nc.scalar.activation(products[:, product_slot(c, h, k), :], src, ACT.Copy,
                                     scale=weight).then_inc(product_ready, 1)

            FIRST_PRODUCTS = [(n, h, PE_TAPS[n][h] + k) for n in PE_TAPS for h in range(HALVES)
                              for k in range(FIRST_POOL_TAPS[n][h])]
            FIRST_PRODUCTS += [(3, i // POOL_TAPS, i % POOL_TAPS) for i in range(PRODUCTS - CARRIED)]

            def multiply_first(first, end):
                for n, h, k in FIRST_PRODUCTS[first:end]:
                    multiply(Chunk(0, n), h, k)

            def absolutes(c):
                act.wait_ge(proj_ready, c.count(1, 1))
                if c.at >= 1:
                    act.wait_ge(y_ready, c.count(2, 0))
                for half, rows in packed:
                    nc.scalar.activation(z_abs[rows, :, :], unpacked(proj_ps[0:N, 0:COLS], half), ACT.Abs,
                                         bias=bp_col[0:N, :]).then_inc(abs_ready, 1)

            def exponential(c):
                act.wait_ge(abs_ready, c.count(2, 2))
                nc.scalar.activation(z_exp[:, :, :], z_abs[:, :, :], ACT.Exp, scale=-1.0).then_inc(exp_ready, 1)

            def squares(c, factors):
                if 0 in factors:
                    act.wait_ge(exp_ready, c.count(1, 1))
                for i in factors:
                    nc.scalar.activation(z_squares[:, i, :, :], z_exp[:, :, :], ACT.Square, scale=SQUARE_SCALE,
                                         bias=shifts[:, i:i + 1]).then_inc(squares_ready, 1)

            def relus(c):
                for half, rows in packed:
                    nc.scalar.activation(z_relu[rows, :, :], unpacked(proj_ps[0:N, 0:COLS], half), ACT.Relu,
                                         bias=bp_col[0:N, :]).then_inc(relu_ready, 1)

            def inputs(c):
                for half, rows in packed:
                    nc.scalar.activation(u_sb[rows, :, :], unpacked(proj_ps[0:N, COLS:2 * COLS], half),
                                         ACT.Identity, bias=bs_col[0:N, :]).then_inc(u_ready, 1)

            def tanhs(c):
                for half, rows in packed:
                    last = nc.scalar.activation(c_tanh[rows, :, :], unpacked(proj_ps[N:P, 0:COLS], half),
                                                ACT.Tanh, bias=bp_col[N:P, :])
                    last.then_inc(tanh_ready, 1)

            evacuate(Chunk(0, 0), 0)
            evacuate(Chunk(0, 0), 1)
            act.wait_ge(taps_ready, 1)
            nc.scalar.activation(hT[:, RING - 1, :, COLS - B:COLS], taps[:, :, 0:TAPS], ACT.Copy).then_inc(h_ready, 1)
            evacuate(Chunk(0, 1), 0)
            evacuate(Chunk(0, 1), 1)
            act.wait_ge(vectors_ps_ready, 1)
            nc.scalar.activation(columns[:, after:], out_ps[1][:, 0:4], ACT.Copy).then_inc(vectors_ready, 1)
            act.wait_ge(vectors_ready, 1)
            nc.scalar.activation(logs_abs[:, :], logs, ACT.Abs).then_inc(logs_act, 1)
            act.wait_ge(logs_act, 1)
            nc.scalar.activation(logs_exp[:, :], logs_abs[:, :], ACT.Exp, scale=-1.0).then_inc(logs_act, 1)
            act.wait_ge(logs_act, 2)
            for i in range(len(LOG1P)):
                nc.scalar.activation(logs_squares[:, i, :], logs_exp[:, :], ACT.Square, scale=SQUARE_SCALE,
                                     bias=shifts[:, i:i + 1]).then_inc(logs_act, 1)
            act.wait_ge(w_in["Wh"], 16)
            nc.scalar.activation(Wh_parts[:, 0, :, :], Wh_sb[:, :, :], ACT.Copy).then_inc(split, 1)
            multiply_first(0, 4)
            act.wait_ge(split, 2)
            nc.scalar.activation(Wh_parts[:, 1, :, :], Wh_rest[:, :, :], ACT.Copy).then_inc(split, 1)
            from_diagonals(1, 0)
            inputs(Chunk(0, 0))
            act.wait_ge(WoT_ps_ready, 1)
            nc.scalar.activation(Wo_boT[:, :, :], out_ps[1][:, 4:4 + HALVES * (N + 1)].rearrange("p (k n) -> p k n", k=HALVES),
                                 ACT.Copy).then_inc(WoT_ready, 1)
            multiply_first(4, 6)
            from_diagonals(1, 1)
            absolutes(Chunk(0, 0))
            exponential(Chunk(0, 0))
            squares(Chunk(0, 0), (0, 1, 2, 3))
            relus(Chunk(0, 0))
            multiply_first(6, 7)
            evacuate(Chunk(0, 2), 0)
            evacuate(Chunk(0, 2), 1)
            tanhs(Chunk(0, 0))
            multiply_first(7, 8)
            act.wait_ge(Wox_ps_ready, 1)
            nc.scalar.activation(Wox[:, :], out_ps[0][0:N + 1, 0:D], ACT.Copy).then_inc(Wox_copied, 1)
            multiply_first(8, 10)
            from_diagonals(2, 0)
            multiply_first(10, 11)
            from_diagonals(2, 1)
            multiply_first(11, 12)

            FIRST_PRODUCTS_AT = [2, 2, 1, 1, 1, 1, 1, 1, 1, 1, 1, 1, 1, 0, 0, 0]
            BEFORE = 12
            assert BEFORE + sum(FIRST_PRODUCTS_AT) == len(FIRST_PRODUCTS)

            def window(c, w):
                for s in range(STEPS):
                    act.wait_ge(mm_ready, c.count(STEPS, s + 1))
                    cols = slice(s * B, (s + 1) * B)
                    nc.scalar.activation(hT[:, c.slot, :, cols], rec_ps[c.pair][:, :, cols], ACT.Tanh).then_inc(h_ready, 1)
                    at = FIRST_AT if w == 0 else USUAL_AT
                    if exists(w, 1):
                        n = c + 1
                        if s == at["absolutes"]:
                            absolutes(n)
                        if s == at["exponential"]:
                            exponential(n)
                        squares(n, at["squares"].get(s, ()))
                        if s == at["relus"]:
                            relus(n)
                        if s == at["inputs"]:
                            inputs(n)
                        if s == at["tanhs"]:
                            tanhs(n)
                    if w == 0:
                        multiply_first(BEFORE + sum(FIRST_PRODUCTS_AT[:s]), BEFORE + sum(FIRST_PRODUCTS_AT[:s + 1]))
                    elif exists(w, 2) and s < CARRIED - 1:
                        for i in range(PRODUCTS - CARRIED + (s + 1 if s else 0), PRODUCTS - CARRIED + s + 2):
                            multiply(c + 2, i // POOL_TAPS, i % POOL_TAPS)
                    if exists(w, 3):
                        if s - at["evacuate"] in (0, 1):
                            evacuate(c + 3, s - at["evacuate"])
                        if w != 0 and s >= CARRIED:
                            multiply(c + 3, (s - CARRIED) // POOL_TAPS, (s - CARRIED) % POOL_TAPS)
                        if (c + 3).slot == RING - 1 and s in (14, 15):
                            history(c + 3, s - 14)
                    if exists(w, -1) and s == 11:
                        store(c + -1, 1)
                    if exists(w, -1) and s == 1:
                        store(c + -1, 0)

            windows(act, window)
            store(Chunk(0, CHUNKS - 1), 0)
            store(Chunk(0, CHUNKS - 1), 1)

        @block.tensor
        def _(pe):
            def transposes(c, j):
                if j == 0:
                    pe.wait_ge(rows_in[c.slot], c.laps(16 * TILES))
                    if c.at >= 1:
                        pe.wait_ge(xt_ready, c.count(HALVES, 0))
                for h in range(HALVES):
                    last = nc.tensor.transpose(xt_ps[:, h * COLS + j * P:h * COLS + (j + 1) * P],
                                               x_rows[:, c.slot, j, h * P:(h + 1) * P], ident[:, :])
                if j == TILES - 1:
                    last.then_inc(xt_ps_ready, 1)

            def xT_of(c, h):
                first = HALO + COLS * c.slot
                return xT[:, h, first:first + COLS]

            def diagonal_taps(n, h):
                pe.wait_ge(diagonals_ready, h + 1)
                pe.wait_ge(xt_ready, n * HALVES + h + 1)
                if n > 1:
                    pe.wait_ge(pool_base[h], n - 1)
                for k in range(PE_TAPS[n][h]):
                    at = HALO + n * COLS + (k - TAPS + 1) * B
                    last = nc.tensor.matmul(rec_ps[1][:, h, (n - 1) * COLS:n * COLS], diagonals[:, h, k, :],
                                            xT[:, h, at:at + COLS], start=k == 0, stop=k == PE_TAPS[n][h] - 1)
                last.then_inc(diagonal_sums, 1)

            def inputs(c, k):
                if k == 0 and c.at >= 1:
                    pe.wait_ge(tanh_ready, c.count(2, 0))
                pe.wait_ge(xt_ready, c.count(HALVES, k + 1))
                nc.tensor.matmul(proj_ps[0:N, COLS:2 * COLS], Ws_sb[:, k, :], xT_of(c, k),
                                 start=k == 0, stop=k == HALVES - 1)

            def project(c, k):
                if k == 0 and c.at == 0 and isinstance(c.lap, int):
                    pe.wait_ge(u_ready, 2)
                pe.wait_ge(conv_ready[k], c.count(1, 1))
                last = nc.tensor.matmul(proj_ps[:, 0:COLS], Wp_sb[:, k, :], conv[:, c.pair, k, :],
                                        start=k == 0, stop=k == HALVES - 1)
                if k == HALVES - 1:
                    last.then_inc(proj_ready, 1)

            ALL, MAIN, REST = slice(0, 256), slice(0, 216), slice(216, 256)

            def drive_x(c, m, k, cols=ALL, start=None):
                if c.at == 1 and isinstance(c.lap, int) and k == 0:
                    pe.wait_ge(pool_base[m], 2)
                nc.tensor.matmul(rec_ps[c.pair][:, m, cols], Wx_sb[:, k, m * P:(m + 1) * P], xT_of(c, k)[:, cols],
                                 start=k == 0 if start is None else start, stop=False, skip_group_check=True)

            def drive_y(c, m):
                if m == 0:
                    pe.wait_ge(y_ready, c.count(2, 2))
                nc.tensor.matmul(rec_ps[c.pair][:, m, 0:COLS], Wox[:, m * P:(m + 1) * P], yT[:, c.slot, :],
                                 start=False, stop=False, skip_group_check=True)

            def out_y(c, j, cols=ALL):
                nc.tensor.matmul(out_ps[j][:, cols], yT[:, c.slot, j * P:(j + 1) * P], Wo_bo[:, cols],
                                 start=cols != REST, stop=False, skip_group_check=True)

            def out_h(c, j):
                pe.wait_ge(h_ready, c.count(STEPS, (j + 1) * TILE_T + 1))
                for m in range(HALVES):
                    last = nc.tensor.matmul(out_ps[j][:, m * P:(m + 1) * P],
                                            hT[:, c.slot, m, j * P:(j + 1) * P], ident[:, :],
                                            is_transpose=True,
                                            start=False, stop=True, skip_group_check=True)
                last.then_inc(out_ps_ready, 1)

            def copies(c, m, s, n):
                bank = (2 * c.pair + m) * BANK
                apart = BANK // 2 - s * B
                return psum[:, bank + s * B:bank + s * B + n * apart].rearrange(
                    "p (d n) -> p d n", n=apart)[:, :, 0:B]

            def step(c, s):
                before = c if s else c + -1
                col = (s - 1) % STEPS * B
                h = [hT[:, before.slot, k, col:col + B] for k in range(HALVES)]
                parts = [[v.bitcast(BF16)[:, 1::2] for v in h],
                         [h_rest[:, s % 2, k, :].bitcast(BF16)[:, 1::2] for k in range(HALVES)],
                         [h_last[:, s % 2, k, :] for k in range(HALVES)]]
                ready = [h_ready, rest_ready, last_ready]
                for p in range(3):
                    pe.wait_ge(ready[p], c.count(STEPS, s + 1))
                    n = 3 if s and p < 2 else 2
                    for m in range(HALVES):
                        for k in range(HALVES):
                            for a in range(3 - p):
                                last = nc.tensor.matmul(copies(c, m, s, n),
                                                        Wh_parts[:, a, k, m * P:(m + 1) * P],
                                                        parts[p][k].unsqueeze(1).broadcast_to([P, n, B]),
                                                        start=False, stop=p == 2 and k == 1, skip_group_check=True)
                last.then_inc(mm_ready, 1)

            pe.wait_ge(ident_ready, 2)
            pe.wait_ge(w_in["cond"], 16)
            pe.wait_ge(w_in["conv_b"], 16)
            for h in range(HALVES):
                last = nc.tensor.transpose(out_ps[0][:, h * (TAPS + 1):(h + 1) * (TAPS + 1)],
                                           cond_rows[:, h * P:(h + 1) * P], ident[0:B + 1, 0:B + 1])
            last.then_inc(taps_ps_ready, 1)
            transposes(Chunk(0, 0), 0)
            transposes(Chunk(0, 0), 1)
            transposes(Chunk(0, 1), 0)
            transposes(Chunk(0, 1), 1)
            pe.wait_ge(w_in["vectors"], 16 * 4)
            nc.tensor.transpose(out_ps[1][:, 0:1], bp_row[:, :], ident[0:1, 0:1])
            for rows in range(2):
                last = nc.tensor.matmul(out_ps[1][rows * N:(rows + 1) * N, 1:4], n_rows[:, :],
                                        ident[0:3, 0:3], start=True, stop=True)
            last.then_inc(vectors_ps_ready, 1)
            pe.wait_ge(w_in["Ws"], 16)
            for k in range(HALVES):
                inputs(Chunk(0, 0), k)
            pe.wait_ge(w_in["Wo"], 16)
            pe.wait_ge(w_in["bo"], 16)
            pe.wait_ge(vectors_ready, 1)
            for h in range(HALVES):
                last = nc.tensor.transpose(out_ps[1][:, 4 + h * (N + 1):4 + (h + 1) * (N + 1)], Wo_bo[:, h * P:(h + 1) * P],
                                           ident[0:N + 1, 0:N + 1])
            last.then_inc(WoT_ps_ready, 1)
            diagonal_taps(1, 0)
            diagonal_taps(1, 1)
            pe.wait_ge(w_in["Wp"], 16)
            for k in range(HALVES):
                project(Chunk(0, 0), k)
            transposes(Chunk(0, 2), 0)
            transposes(Chunk(0, 2), 1)
            pe.wait_ge(w_in["Wx"], 16)
            pe.wait_ge(WoT_ready, 1)
            pe.wait_ge(taps_ready, 1)
            for k in range(HALVES):
                last = nc.tensor.matmul(out_ps[0][0:N + 1, 0:D], Wo_boT[:, k, :], Wx_sb[:, k, :],
                                        start=k == 0, stop=k == HALVES - 1)
            last.then_inc(Wox_ps_ready, 1)
            for m in range(HALVES):
                for k in range(HALVES):
                    drive_x(Chunk(0, 0), m, k)
            diagonal_taps(2, 0)
            diagonal_taps(2, 1)
            pe.wait_ge(Wox_ready, 1)
            pe.wait_ge(cleared, CLEARED)
            for m in range(HALVES):
                drive_y(Chunk(0, 0), m)
            pe.wait_ge(split, SPLITS)

            DRIVE_X_AT = (6, 7, 8, 9)

            def window(c, w):
                for s in range(STEPS):
                    step(c, s)
                    at = FIRST_AT if w == 0 else USUAL_AT
                    if exists(w, 3) and s - at["transposes"] in (0, 1):
                        transposes(c + 3, s - at["transposes"])
                    if w == 0:
                        if s in (1, 2):
                            inputs(c + 1, s - 1)
                        elif s - at["project"] in (0, 1):
                            project(c + 1, s - at["project"])
                        elif s in DRIVE_X_AT:
                            i = DRIVE_X_AT.index(s)
                            drive_x(c + 1, i // 2, i % 2)
                        elif s in (12, 13):
                            inputs(c + 2, s - 12)
                        elif s >= 14:
                            drive_y(c + 1, s - 14)
                    elif exists(w, 1):
                        n = c + 1
                        if s - at["project"] in (0, 1):
                            project(n, s - at["project"])
                        elif 6 <= s < 10:
                            if s < 8:
                                drive_x(n, 0, s - 6, MAIN, start=False)
                            else:
                                drive_x(n, 1, s - 8)
                        elif s >= 14:
                            drive_y(n, s - 14)
                        if s in (4, 5):
                            drive_x(n, 0, s - 4, REST, start=s == 4)
                        if exists(w, 2) and s in (12, 13):
                            inputs(c + 2, s - 12)
                    if exists(w, -1):
                        if s == 2:
                            out_y(c + -1, 1, MAIN)
                        if s == 3:
                            out_y(c + -1, 1, REST)
                            out_h(c + -1, 1)
                    if s == 10:
                        out_y(c, 0, MAIN)
                    if s == 11:
                        out_y(c, 0, REST)
                        out_h(c, 0)

            windows(pe, window)
            out_y(Chunk(0, CHUNKS - 1), 1)
            out_h(Chunk(0, CHUNKS - 1), 1)

        @block.vector
        def _(dve):
            for k in range(RING):
                dve.sem_inc(stored[k], 16)
            nc.vector.memset(yT[N:N + 1, :, :], 1.0).then_inc(cleared, 1)
            nc.vector.memset(decays[:, :, 1:], 1.0).then_inc(cleared, 1)
            nc.vector.memset(decays[:, :, 0], 0.0).then_inc(cleared, 1)
            nc.vector.memset(state[:, 1, :, :], 0.0).then_inc(cleared, 1)

            def first_taps(h, k):
                start = (TAPS - 1 - k) * B
                acc = conv[:, 0, h, start:COLS]
                src = xT[:, h, HALO:HALO + COLS - start]
                weight = taps[:, h, k:k + 1]
                if k == TAPS - 1:
                    dve.wait_ge(xt_ready, h + 1)
                    ins = nc.vector.tensor_scalar(acc, src, weight, conv_bT[:, h:h + 1], ALU.mult, ALU.add)
                else:
                    dve.wait_ge(conv_step[h], TAPS - 1 - k)
                    ins = nc.vector.scalar_tensor_tensor(out=acc, in0=src, scalar=weight, in1=acc,
                                                         op0=ALU.mult, op1=ALU.add)
                ins.then_inc(conv_step[h] if k else conv_ready[h], 1)

            def taps_of(c, h, k):
                acc = conv[:, c.pair, h, :]
                at = HALO + COLS * c.slot + (k - TAPS + 1) * B
                src = xT[:, h, at:at + COLS]
                weight = taps[:, h, k:k + 1]
                if k == dve_first(c, h):
                    if c.slot == 0 and c.at >= RING:
                        dve.wait_ge(halo_ready, c.laps(HALVES, -1))
                    dve.wait_ge(pool_step, sums_before(c, h, k - 1)(1))
                    so_far = pool_conv[:, c.pair, h, :]
                else:
                    dve.wait_ge(conv_step[h], dve_taps_before(c, h, k))
                    so_far = acc
                ins = nc.vector.scalar_tensor_tensor(out=acc, in0=src, scalar=weight, in1=so_far,
                                                     op0=ALU.mult, op1=ALU.add)
                ins.then_inc(conv_ready[h] if k == TAPS - 1 else conv_step[h], 1)

            def tail(c, i):
                n = len(LOG1P)
                s_now, s_old = state[:, c.pair, :, :], state[:, 1 - c.pair, :, :]
                if 0 < i <= CHAIN:
                    dve.wait_ge(tail_step, c.count(CHAIN, i))
                if i < n:
                    dve.wait_ge(squares_ready, c.count(n, i + 1))
                    so_far = drive if i else z_exp
                    nc.vector.scalar_tensor_tensor(out=drive[:, :, :], in0=z_squares[:, i, :, :], scalar=LOG1P[i][1],
                                                   in1=so_far[:, :, :], op0=ALU.add, op1=ALU.mult).then_inc(tail_step, 1)
                elif i == n:
                    dve.wait_ge(relu_ready, c.count(2, 2))
                    nc.vector.tensor_tensor(drive[:, :, :], drive[:, :, :], z_relu[:, :, :], ALU.add).then_inc(tail_step, 1)
                elif i == n + 1:
                    dve.wait_ge(u_ready, c.count(2, 2))
                    nc.vector.tensor_tensor(drive[:, :, :], drive[:, :, :], u_sb[:, :, :], ALU.mult).then_inc(tail_step, 1)
                elif i == n + 2:
                    nc.vector.scalar_tensor_tensor(out=drive[:, :, 0], in0=s_old[:, :, STEPS - 1], scalar=decay[:, :],
                                                   in1=drive[:, :, 0], op0=ALU.mult, op1=ALU.add).then_inc(tail_step, 1)
                elif i == n + 3:
                    nc.vector.tensor_tensor_scan(s_now.rearrange("p b t -> p (b t)"),
                                                 decays[:, :, :].rearrange("p b t -> p (b t)"),
                                                 drive[:, :, :].rearrange("p b t -> p (b t)"),
                                                 0.0, ALU.mult, ALU.add).then_inc(tail_step, 1)
                else:
                    half = i - CHAIN
                    rows = packed[half][1]
                    if half == 0:
                        dve.wait_ge(tanh_ready, c.count(2, 2))
                    nc.vector.scalar_tensor_tensor(out=unpacked(yT[0:N, c.slot, :], half), in0=c_tanh[rows, :, :],
                                                   scalar=logs_sp[rows, 1:2], in1=s_now[rows, :, :],
                                                   op0=ALU.mult, op1=ALU.mult).then_inc(y_ready, 1)

            TAIL = CHAIN + 2

            def state_parts(g, h, q):
                dve.wait_ge(h_ready, g)
                rest = h_rest[:, q, :, :]
                nc.vector.tensor_tensor(rest, h, h.bitcast(BF16)[:, :, 1::2], ALU.subtract).then_inc(rest_ready, 1)
                dve.wait_ge(rest_ready, g)
                nc.vector.tensor_tensor(h_last[:, q, :, :], rest, rest.bitcast(BF16)[:, :, 1::2],
                                        ALU.subtract).then_inc(last_ready, 1)

            def add_x(c, j):
                k = 2 * c.pair + j
                dve.wait_ge(out_ps_ready, c.count(TILES, j + 1))
                if j == 0:
                    dve.wait_ge(again_in[c.slot], c.laps(16 * TILES))
                dve.wait_ge(stored[k], stores_before(c))
                nc.vector.tensor_tensor(out_rows[:, k, :], out_ps[j][:, 0:D], x_again[:, c.slot, j, :],
                                        ALU.add).then_inc(out_ready, 1)

            dve.wait_ge(taps_ready, 1)
            dve.wait_ge(cleared, CLEARED)
            n_factors = len(LOG1P)

            def set_up(i):
                if i:
                    dve.wait_ge(consts, i)
                if i < n_factors:
                    dve.wait_ge(logs_act, i + 3)
                    so_far = logs_sp if i else logs_exp
                    ins = nc.vector.scalar_tensor_tensor(out=logs_sp[:, :], in0=logs_squares[:, i, :], scalar=LOG1P[i][1],
                                                         in1=so_far[:, :], op0=ALU.add, op1=ALU.mult)
                elif i == n_factors:
                    ins = nc.vector.scalar_tensor_tensor(out=logs_sp[:, :], in0=logs, scalar=0.0, in1=logs_sp[:, :],
                                                         op0=ALU.max, op1=ALU.add)
                elif i == n_factors + 1:
                    ins = nc.vector.tensor_tensor(dt_A[:, :], logs_sp[:, 0:1], logs_sp[:, 1:2], ALU.mult)
                elif i == n_factors + 2:
                    ins = nc.vector.tensor_scalar(decay[:, :], dt_A[:, :], -1.0, 1.0, ALU.mult, ALU.add)
                elif i == n_factors + 3:
                    ins = nc.vector.tensor_scalar(decays[:, :, :], decays[:, :, :], decay[:, :], None, ALU.mult)
                ins.then_inc(consts, 1)

            SET_UP = n_factors + 4
            for k in reversed(range(TAPS)):
                for h in range(HALVES):
                    first_taps(h, k)
            dve.wait_ge(vectors_ready, 1)
            for i in range(SET_UP):
                set_up(i)
            dve.wait_ge(consts, SET_UP)
            state_parts(1, hT[:, RING - 1, :, COLS - B:COLS], 0)
            one_0, one_1, two_0, two_1 = [[(n, h, k) for k in range(dve_first(Chunk(0, n), h), TAPS)]
                                          for n in PE_TAPS for h in range(HALVES)]
            FIRST_TAPS = one_0 + one_1 + two_0[:3]
            for i in range(5):
                FIRST_TAPS += [two_0[3 + i], two_1[i]]
            FIRST_TAPS += two_1[5:]
            IN_TAIL = 4
            FIRST_TAPS_AT = [9, 2, 2, 2, 1, 1, 2, 2, 1, 1, 1, 1, 1, 0, 1, 2, 1]
            assert sum(FIRST_TAPS_AT) == len(FIRST_TAPS)

            for i in range(TAIL):
                tail(Chunk(0, 0), i)
                if 1 <= i <= IN_TAIL:
                    taps_of(Chunk(0, 1), *FIRST_TAPS[i - 1][1:])
            dve.wait_ge(Wox_copied, 1)
            dve.wait_ge(w_in["b"], 16)
            nc.vector.tensor_tensor(Wox[N:N + 1, :], Wox[N:N + 1, :], b_row[N:N + 1, :], ALU.add).then_inc(Wox_ready, 1)
            for n, h, k in FIRST_TAPS[IN_TAIL:FIRST_TAPS_AT[0]]:
                taps_of(Chunk(0, n), h, k)

            TAPS_AT = [(1, 0)] * 7 + [(0, 1)] * 5 + [(0, 0), (0, 1), (1, 1), (0, 1)]
            assert [sum(n[h] for n in TAPS_AT) for h in range(HALVES)] == [TAPS - POOL_TAPS] * HALVES

            def window(c, w):
                tap = [POOL_TAPS] * HALVES
                for s in range(STEPS):
                    state_parts(c.count(STEPS, s + 2), hT[:, c.slot, :, s * B:(s + 1) * B], (s + 1) % 2)
                    steps_of_tail = (FIRST_AT if w == 0 else USUAL_AT)["tail"].get(s, ()) if exists(w, 1) else ()
                    for i in steps_of_tail[:1]:
                        tail(c + 1, i)
                    if w == 0:
                        for n, h, k in FIRST_TAPS[sum(FIRST_TAPS_AT[:s + 1]):sum(FIRST_TAPS_AT[:s + 2])]:
                            taps_of(Chunk(0, n), h, k)
                    elif exists(w, 2):
                        for h in range(HALVES):
                            for _ in range(TAPS_AT[s][h]):
                                taps_of(c + 2, h, tap[h])
                                tap[h] += 1
                    for i in steps_of_tail[1:]:
                        tail(c + 1, i)
                    if exists(w, -1) and s == 4:
                        add_x(c + -1, 1)
                    if s == (15 if w == 0 else 13):
                        add_x(c, 0)

            windows(dve, window)
            add_x(Chunk(0, CHUNKS - 1), 1)


def kernel(x, cond_1024, L0_cond_conv_b, L0_cond_Wp, L0_cond_bp, L0_cond_Ws, L0_cond_bs, L0_cond_A_log,
           L0_cond_dt_log, L0_cond_Wo, L0_cond_bo, L1_cond_Wx, L1_cond_Wh, L1_cond_b):
    import numpy as np
    import concourse.bacc as bacc
    from concourse.bass_utils import run_bass_kernel_spmd

    given = dict(x=x, cond=cond_1024, conv_b=L0_cond_conv_b, Wp=L0_cond_Wp, bp=L0_cond_bp, Ws=L0_cond_Ws,
                 bs=L0_cond_bs, A_log=L0_cond_A_log, dt_log=L0_cond_dt_log, Wo=L0_cond_Wo, bo=L0_cond_bo,
                 Wx=L1_cond_Wx, Wh=L1_cond_Wh, b=L1_cond_b)
    nc = bacc.Bacc("TRN2", target_bir_lowering=False, num_devices=1)
    arrays, args = {}, {}
    for name, a in given.items():
        a = np.ascontiguousarray(a)
        arrays[f"in_{name}"] = a
        args[name] = nc.dram_tensor(f"in_{name}", a.shape, mybir.dt.from_np(a.dtype), kind="ExternalInput").ap()
    args["out"] = nc.dram_tensor("out_dram", x.shape, FP32, kind="ExternalOutput").ap()
    build(nc, **args)
    r = run_bass_kernel_spmd(nc, [arrays], core_ids=[0])
    return r.results[0]["out_dram"]
```
